# Optimizing a Trainium2 kernel written in Bass

```python
import numpy as np
import jax
import jax.numpy as jnp

def _softmax(x, axis=-1):
    return jax.nn.softmax(x, axis=axis)

def _gelu(x):
    return jax.nn.gelu(x, approximate=True)

def _silu(x):
    return jax.nn.silu(x)

def _sigmoid(x):
    return jax.nn.sigmoid(x)

def _layernorm(x, axis=-1, eps=1e-05):
    m = jnp.mean(x, axis=axis, keepdims=True)
    v = jnp.var(x, axis=axis, keepdims=True)
    return (x - m) / jnp.sqrt(v + eps)

def _scatter_add(tgt, idx, src, axis=0):
    return tgt.at[idx].add(src)

def _segment_sum(src, seg, n):
    return jax.ops.segment_sum(src, seg, n)
kernel_name = 'mk_macaron_d1_jaxref_r2_2e8390'

def setup_inputs(seed: int=0):
    np.random.seed(seed)
    _w = jnp.asarray

    def _L0_attn_setup():
        import math
        import jax, jax.numpy as jnp
        import numpy as np
        B_SZ, L, D_EXP, D_RANK, N = (2, 1024, 512, 64, 16)
        DT_MIN, DT_MAX = (0.001, 0.1)
        key = jax.random.key(seed)
        k0, k1, k2, k3 = jax.random.split(key, 4)
        x = jax.random.normal(k0, (B_SZ, L, D_EXP), jnp.float32)
        x_proj_w = jax.random.normal(k1, (D_RANK + 2 * N, D_EXP), jnp.float32) / jnp.sqrt(jnp.float32(D_EXP))
        x_proj_b = jnp.zeros((D_RANK + 2 * N,), jnp.float32)
        std = 1.0 / np.sqrt(D_RANK)
        dt_proj_w = jax.random.uniform(k2, (D_EXP, D_RANK), jnp.float32, -std, std)
        dt = jnp.exp(jax.random.uniform(k3, (D_EXP,), jnp.float32) * (np.log(DT_MAX) - np.log(DT_MIN)) + np.log(DT_MIN))
        dt = jnp.clip(dt, DT_MIN, None)
        dt_proj_b = dt + jnp.log(-jnp.expm1(-dt))
        A_log = jnp.log(jnp.broadcast_to(jnp.arange(1, N + 1, dtype=jnp.float32), (D_EXP, N)))
        return {'x': x, 'x_proj_w': x_proj_w, 'x_proj_b': x_proj_b, 'dt_proj_w': dt_proj_w, 'dt_proj_b': dt_proj_b, 'A_log': A_log}
    _L0_attn_in = _L0_attn_setup()

    def _L0_ffn_setup():
        import jax, jax.numpy as jnp
        import numpy as np
        DIM = 512

        def _reference_tuple_inner(x, W_r, W_k, W_v, mu_r, mu_k):
            B, T, C = x.shape
            x_prev = jnp.concatenate([jnp.zeros((B, 1, C), x.dtype), x[:, :-1, :]], axis=1)
            xr = mu_r * x + (1.0 - mu_r) * x_prev
            xk = mu_k * x + (1.0 - mu_k) * x_prev
            r = jax.nn.sigmoid(jnp.einsum('btc,dc->btd', xr, W_r))
            k = jnp.einsum('btc,dc->btd', xk, W_k)
            k_act = jnp.square(jax.nn.relu(k))
            out = r * jnp.einsum('btc,dc->btd', k_act, W_v)
            new_state = x[:, -1, :]
            return (out, new_state)
        key = jax.random.key(seed)
        ks = jax.random.split(key, 6)
        B, T, C = (8, 1024, DIM)
        x = jax.random.normal(ks[0], (B, T, C), dtype=jnp.float32)
        s = 1.0 / np.sqrt(C)
        W_r = jax.random.uniform(ks[1], (C, C), jnp.float32, -s, s)
        W_k = jax.random.uniform(ks[2], (C, C), jnp.float32, -s, s)
        W_v = jax.random.uniform(ks[3], (C, C), jnp.float32, -s, s)
        mu_r = jax.random.uniform(ks[4], (C,), jnp.float32)
        mu_k = jax.random.uniform(ks[5], (C,), jnp.float32)
        return {'x': x, 'W_r': W_r, 'W_k': W_k, 'W_v': W_v, 'mu_r': mu_r, 'mu_k': mu_k}
    _L0_ffn_in = _L0_ffn_setup()
    _d = {'L0_attn_x': _L0_attn_in['x'], 'L0_attn_x_proj_w': _L0_attn_in['x_proj_w'], 'L0_attn_x_proj_b': _L0_attn_in['x_proj_b'], 'L0_attn_dt_proj_w': _L0_attn_in['dt_proj_w'], 'L0_attn_dt_proj_b': _L0_attn_in['dt_proj_b'], 'L0_attn_A_log': _L0_attn_in['A_log'], 'L0_ffn_W_r': _L0_ffn_in['W_r'], 'L0_ffn_W_k': _L0_ffn_in['W_k'], 'L0_ffn_W_v': _L0_ffn_in['W_v'], 'L0_ffn_mu_r': _L0_ffn_in['mu_r'], 'L0_ffn_mu_k': _L0_ffn_in['mu_k']}
    _x0 = _d['L0_attn_x']
    _d['L0_attn_x'] = jax.random.normal(jax.random.fold_in(jax.random.key(seed), 1), (8, 2048, 512), dtype=_x0.dtype)
    del _x0
    return _d

def reference(L0_attn_x, L0_attn_x_proj_w, L0_attn_x_proj_b, L0_attn_dt_proj_w, L0_attn_dt_proj_b, L0_attn_A_log, L0_ffn_W_r, L0_ffn_W_k, L0_ffn_W_v, L0_ffn_mu_r, L0_ffn_mu_k):

    def _L0_attn_ref(x, x_proj_w, x_proj_b, dt_proj_w, dt_proj_b, A_log):
        import math
        import jax, jax.numpy as jnp
        import numpy as np
        B_SZ, L, D_EXP, D_RANK, N = (2, 1024, 512, 64, 16)
        DT_MIN, DT_MAX = (0.001, 0.1)
        proj = x @ x_proj_w.T + x_proj_b
        dt_r, Bm, C = jnp.split(proj, [D_RANK, D_RANK + N], axis=-1)
        dt = jax.nn.softplus(dt_r @ dt_proj_w.T + dt_proj_b)
        A = -jnp.exp(A_log)
        dA = jnp.exp(jnp.einsum('bld,dn->bldn', dt, A))
        dBX = (dt * x)[..., None] * Bm[:, :, None, :]
        for i in range(int(math.log2(x.shape[1]))):
            s = 2 ** i
            new_dBX = jnp.concatenate([dBX[:, :s], dA[:, s:] * dBX[:, :-s] + dBX[:, s:]], axis=1)
            new_dA = jnp.concatenate([dA[:, :s], dA[:, s:] * dA[:, :-s]], axis=1)
            dA, dBX = (new_dA, new_dBX)
        return jnp.einsum('bldn,bln->bld', dBX, C)

    def _L0_ffn_ref(x, W_r, W_k, W_v, mu_r, mu_k):
        import jax, jax.numpy as jnp
        import numpy as np
        DIM = 512

        def _reference_tuple_inner(x, W_r, W_k, W_v, mu_r, mu_k):
            B, T, C = x.shape
            x_prev = jnp.concatenate([jnp.zeros((B, 1, C), x.dtype), x[:, :-1, :]], axis=1)
            xr = mu_r * x + (1.0 - mu_r) * x_prev
            xk = mu_k * x + (1.0 - mu_k) * x_prev
            r = jax.nn.sigmoid(jnp.einsum('btc,dc->btd', xr, W_r))
            k = jnp.einsum('btc,dc->btd', xk, W_k)
            k_act = jnp.square(jax.nn.relu(k))
            out = r * jnp.einsum('btc,dc->btd', k_act, W_v)
            new_state = x[:, -1, :]
            return (out, new_state)
        return _reference_tuple_inner(x, W_r, W_k, W_v, mu_r, mu_k)[0]
    x = L0_attn_x
    x = x + 0.5 * _L0_ffn_ref(_layernorm(x, axis=-1), L0_ffn_W_r, L0_ffn_W_k, L0_ffn_W_v, L0_ffn_mu_r, L0_ffn_mu_k)
    x = x + _L0_attn_ref(_layernorm(x, axis=-1), L0_attn_x_proj_w, L0_attn_x_proj_b, L0_attn_dt_proj_w, L0_attn_dt_proj_b, L0_attn_A_log)
    x = x + 0.5 * _L0_ffn_ref(_layernorm(x, axis=-1), L0_ffn_W_r, L0_ffn_W_k, L0_ffn_W_v, L0_ffn_mu_r, L0_ffn_mu_k)
    return x

_drawn_inputs = setup_inputs


def setup_inputs(seed=0):
    import zlib

    import numpy as np

    out = dict(_drawn_inputs(seed))
    spreads = {'L0_attn_x_proj_b': (0.0, 0.1)}
    factors = {'L0_ffn_W_r': 3.24, 'L0_ffn_mu_r': 6.616}
    for name, (base, spread) in spreads.items():
        noise = np.random.default_rng([zlib.crc32(name.encode()), seed]).standard_normal(out[name].shape)
        drawn = base * np.exp(spread * noise) if base else spread * noise
        out[name] = jnp.asarray(drawn.astype(out[name].dtype))
    for name, factor in factors.items():
        out[name] = (out[name] * factor).astype(out[name].dtype)
    return out
```

```python
from contextlib import ExitStack

import concourse.bass as bass
from concourse import mybir

F32 = mybir.dt.float32
ALU = mybir.AluOpType
ACT = mybir.ActivationFunctionType

P = 128
T = 512
TT = T // P
D = 512
DG = D // P
N = 16
RANK = 64
PROJ = RANK + 2 * N
EPS = 1e-5
RING = 4
BG = 4

PER_BATCH = 4
WEIGHTS_LOADED = 16 * 11
AHEAD = 1
SUM_LATER = 4
PHASES = 4 * N


def some(piece, lag, *ks):
    return [(piece, k, lag) for k in ks]


ORDER = (some("K1", 0, 3) + some("R1", 0, 0, 1, 2, 3)
         + some("V1", 0, 0) + some("T2", 2, 0) + some("V1", 0, 1) + some("T2", 2, 1, 2)
         + some("V1", 0, 2) + some("T2", 2, 3) + some("V1", 0, 3)
         + some("K2", 2, 0, 1, 2, 3)
         + some("R2", 2, 0) + some("Z", 0, 0, 1) + some("R2", 2, 1) + some("Z", 0, 2, 3) + some("R2", 2, 2)
         + some("P", 0, 0) + some("R2", 2, 3) + some("C", 0, 0) + some("D", 0, 0, 1, 2, 3)
         + some("V2", 2, 0) + some("T1", -1, 0) + some("V2", 2, 1) + some("T1", -1, 1, 2)
         + some("V2", 2, 2) + some("T1", -1, 3) + some("V2", 2, 3)
         + some("K1", -1, 0, 1, 2))
PE_COST = {"T": 0.5, "Z": 0.5, "C": 1.2}
PE_STEPS = {"T": 1, "Z": 1, "K": DG, "R": DG, "V": DG, "P": DG, "C": 1, "D": 1}
ACT_STEPS = {"T": 2, "Z": 1, "K": 2, "R": 1, "V": 0, "P": 2, "C": 1, "D": 2}
LATER = dict(T=0, Z=1, K=1, R=1, V=0, P=1, C=0, D=0, mix=1)
STATS_SLOT = 9
KIND = {"1": 0, "2": 1, "Z": 2}
LAGS = range(-1, 4)


def timetable():
    pe, act, dve = ([[] for _ in range(PHASES)] for _ in range(3))
    pool = [[] for _ in range(N)]
    begun_at, filled_at, read_at, normed_at = {}, {}, {}, {}
    steps = [(lag, p, k, s) for p, k, lag in ORDER for s in range(PE_STEPS[p[0]])]
    costs = [PE_COST.get(p[0], 1.0) for _, p, _, _ in steps]
    for r, (lag, p, k, s) in enumerate(steps):
        phase = int(PHASES * sum(costs[:r]) / sum(costs))
        pe[phase].append((lag, p, k, s))
        begun_at.setdefault((p, k), lag * PHASES + phase)
        filled_at[p, k] = lag * PHASES + phase
    in_turn = sorted(filled_at, key=lambda piece: filled_at[piece] % PHASES)

    def place(table, at, *what, most=2):
        while len(table[at % PHASES]) >= most:
            at += 1
        table[at % PHASES].append((at // PHASES,) + what)
        return at

    def give_pool(at, what, k):
        slot = at // 4 + 1
        pool[slot % N].append((slot // N, what, k, 0))
        return 4 * slot - 1

    for p, k in in_turn:
        at = filled_at[p, k] + LATER[p[0]]
        for s in range(ACT_STEPS[p[0]]):
            at = place(act, at + (p[0] == "K" and s == 1), p, k, s)
        read_at[p, k] = at
    for g in range(DG):
        read_at["E", g] = place(act, read_at["D", g] + 1, "E", g, 0)
    at = max(read_at["E", g] for g in range(DG)) + 1
    act[at % PHASES].insert(0, (at // PHASES, "L", 0, 0))
    give_pool(at, "dt", 0)
    for p, k in in_turn:
        if p[0] == "T":
            for s in range(2):
                read_at[p, k] = place(dve, read_at[p, k] + LATER["mix"] * (s == 0), p, k, s)
        if p[0] == "V":
            at = place(dve, max(filled_at[p, k], read_at["R" + p[1], k]) + LATER["V"], p, k, 0)
            read_at[p, k] = give_pool(at, "A" + p[1], k)
    for kind, at in (("2", 2 * PHASES + SUM_LATER), ("Z", read_at["V1", TT - 1] + 1), ("1", -PHASES + 4 * STATS_SLOT)):
        for s in range(TT + 1):
            if kind == "Z" and s < TT:
                at = read_at["V1", s] + 1
            at = place(dve, at, "S" + kind, 0, s)
        at = give_pool(at, "N" + kind, 0) + 2
        for s in range(TT):
            at = place(act, at, "N" + kind, 0, s, most=3)
        normed_at[kind] = at
    check_order(begun_at, filled_at, read_at, normed_at)
    return pe, act, dve, pool


def check_order(begun_at, filled_at, read_at, normed_at):
    for piece in ("T1", "T2", "Z"):
        kind = piece[-1]
        assert begun_at[piece, 0] > normed_at[kind], (piece, begun_at[piece, 0], normed_at[kind])
    for before, after, wrap in (("T2", "Z", 2), ("Z", "1", 1), ("T1", "2", -2)):
        gap = normed_at[after] - TT - filled_at[before, DG - 1] + wrap * PHASES
        assert gap > 0, (before, after, gap)
    for which in "12":
        assert begun_at["K" + which, 0] > max(read_at["T" + which, g] for g in range(DG)), ("K", which)
        assert begun_at["V" + which, 0] > max(read_at["K" + which, g] for g in range(DG)), ("V", which)
    assert begun_at["P", 0] > max(read_at["Z", g] for g in range(DG))
    assert filled_at["C", 0] > read_at["P", 0]
    flat = [(p, k) for p, k, _ in ORDER]
    for new, old in zip(flat, flat[-RING:] + flat[:-RING]):
        begun = begun_at[new] % PHASES
        read = filled_at[old] % PHASES + read_at[old] - filled_at[old]
        assert begun + PHASES * (filled_at[old] % PHASES > begun) >= read, (new, old)


class Step:

    def __init__(self, i, turn, chunks):
        self.i, self.turn, self.chunks = i, turn, chunks

    def has(self, lag):
        return 0 <= self.i - lag < self.chunks

    def due(self, entries):
        return [(p, k, s, self.i - lag) for lag, p, k, s in entries if self.has(lag)]


def bank_table(chunks):
    table = {}
    for i in range(-1, chunks + 3):
        for piece, k, lag in ORDER:
            if 0 <= i - lag < chunks:
                table[i - lag, piece, k] = len(table)
    return table


def macaron_kernel(nc, x, ident, wr_t, wk_t, wv_t, mu_r, mu_k, xp_t, xp_b, dt_t, dt_b, a_log, scratch, out):
    chunks = x.shape[0]
    fills = bank_table(chunks)
    pe_share, act_share, dve_share, pool_share = timetable()
    fills_per_chunk = len(ORDER)
    assert chunks % PER_BATCH == 0 and chunks >= 8 and (PER_BATCH * fills_per_chunk) % RING == 0

    with ExitStack() as ctx:
        def sb(name, shape):
            return ctx.enter_context(nc.sbuf_tensor(name, shape, F32))

        def ps(name, shape):
            return ctx.enter_context(nc.psum_tensor(name, shape, F32))

        rates = {}

        def sem(name, per_chunk=0):
            semaphore = ctx.enter_context(nc.semaphore(name))
            rates[semaphore.name] = per_chunk
            return semaphore

        eye = sb("eye", [P, P])
        w_r = sb("w_r", [P, DG, D])
        w_k = sb("w_k", [P, DG, D])
        w_v = sb("w_v", [P, DG, D])
        w_x = sb("w_x", [P, DG, PROJ])
        w_dt = sb("w_dt", [RANK + 1, D])
        b_x = sb("b_x", [PROJ, 1])
        mu = sb("mu", [P, 2, DG])
        one_mu = sb("one_mu", [P, 2, DG])
        neg_a = sb("neg_a", [P, DG, N])
        zero = sb("zero", [P, DG])
        eps = sb("eps", [P, TT])
        minus_half = sb("minus_half", [P, TT])
        minus_one = sb("minus_one", [P, TT])
        ones = sb("ones", [P, DG])

        xs = sb("xs", [P, RING, TT, D])
        xn = sb("xn", [P, TT, D])
        mixed = sb("mixed", [P, 2, 2, DG, T + 1])
        key = sb("key", [P, DG, T])
        gate = sb("gate", [P, TT, D])
        gated = sb("gated", [P, 2, D])
        z_t = sb("z_t", [P, DG, T])
        dt_r = sb("dt_r", [RANK + 1, T])
        bc_t = sb("bc_t", [2 * N, T])
        bc_tok = sb("bc_tok", [P, 2, TT, 2 * N])
        dt = sb("dt", [P, 2, DG, T])
        u = sb("u", [P, DG, T])
        relu_z = mixed[:, 1, 1, :, 0:T]
        b_all = sb("b_all", [P, 2, BG, T])
        dbx = sb("dbx", [P, 2, DG, T])
        h = sb("h", [P, 2, DG, T])
        state = sb("state", [P, N, DG])
        stats = sb("stats", [P, 3, TT, 6])
        mean_var = sb("mean_var", [P, 3, TT, 2])
        rstd = sb("rstd", [P, 3, TT])
        shift = sb("shift", [P, 3, TT])
        spare = sb("spare", [P, 1])

        ring = ps("ring", [P, RING, 512])
        dec = ps("dec", [P, 2, 512])
        h_tok = ps("h_tok", [P, 2, 512])

        weights_in = sem("weights_in")
        consts = sem("consts")
        a_exp = sem("a_exp")
        x_in = [sem(f"x_in{b}", 4) for b in range(RING)]
        stored = sem("stored", 16)
        scratch_in = sem("scratch_in", 32)
        b_in = [sem(f"b_in{b}", 32) for b in range(2)]
        filled = sem("filled", fills_per_chunk)
        done = [sem(f"done{b}", fills_per_chunk / RING) for b in range(RING)]
        bn_done = [sem(f"bn_done{k}", TT) for k in range(3)]
        stats_ready = [sem(f"stats_ready{k}", TT) for k in range(3)]
        small = [sem(f"small{k}", 4) for k in range(3)]
        normed = [sem(f"normed{k}", TT) for k in range(3)]
        turned = sem("turned", 2 * DG)
        carried = sem("carried", 2)
        squared = sem("squared", 2 * DG)
        x_added = sem("x_added", 2 * TT)
        exp_done = sem("exp_done", DG)
        log_done = sem("log_done", DG)
        dt_ready = sem("dt_ready", DG)
        u_ready = sem("u_ready", DG)
        dbx_ready = sem("dbx_ready", N)
        saved = sem("saved", N)
        dec_ready = sem("dec_ready", N * DG)
        scanned = sem("scanned", N * DG)
        h_turned = sem("h_turned", N * TT)
        summed = sem("summed", N * TT)

        def count(it, semaphore, value):
            if it.turn is None:
                return value if value > 0 else None
            assert value > 0 and rates[semaphore.name] > 0
            return it.turn * int(PER_BATCH * rates[semaphore.name]) + value

        def ffn_number(kind, j):
            if kind == 0:
                return j if j <= 2 else 2 * j - 2
            return min(2 * j + 3, chunks + j)

        def bank(j, piece, k):
            return fills[j, piece, k] % RING

        def bank_filled(it, j, piece, k):
            return filled, count(it, filled, fills[j, piece, k] + 1)

        def read_through(it, j, piece, k):
            b = bank(j, piece, k)
            return done[b], count(it, done[b], fills[j, piece, k] // RING + 1)

        def transposed_before(it, phase):
            last = 0
            for i in (it.i - 1, it.i):
                for entries in pe_share[:phase if i == it.i else PHASES]:
                    for lag, piece, k, _ in entries:
                        if piece[0] in "TZ" and (i - lag, piece, k) in fills:
                            last = fills[i - lag, piece, k] + 1
            return last

        def program(eng, body):
            for i in range(-1, 3):
                body(Step(i, None, chunks))
            with eng.Fori(0, (chunks - PER_BATCH) // PER_BATCH) as turn:
                for i in range(3, 3 + PER_BATCH):
                    body(Step(i, turn, chunks))
            for i in range(chunks - 1, chunks + 3):
                body(Step(i, None, chunks))

        block = ctx.enter_context(nc.Block())

        @block.sync
        def _(sp):
            for dst, src in ((eye[:], ident), (mu[:, 0], mu_r), (mu[:, 1], mu_k), (b_x[:], xp_b),
                             (neg_a[:], a_log), (w_k[:], wk_t), (w_r[:], wr_t), (w_v[:], wv_t), (w_x[:], xp_t),
                             (w_dt[0:RANK, :], dt_t), (w_dt[RANK:RANK + 1, :], dt_b)):
                sp.dma_start(dst, src).then_inc(weights_in, 16)

            def load_b(j, group):
                half = group % 2
                rows = scratch[j % 2, BG * group:BG * (group + 1), :].unsqueeze(0).broadcast_to([P, BG, T])
                sp.dma_start(b_all[:, half], rows).then_inc(b_in[half], 16)

            def dram_chunk(tensor, it, j):
                chunk = tensor[j] if it.turn is None else tensor[it.turn * PER_BATCH + j]
                return chunk.rearrange("(t p) d -> p t d", p=P)

            def body(it):
                if it.has(3):
                    j = it.i - 3
                    sp.wait_ge(x_added, count(it, x_added, TT * (ffn_number(1, j) + 1)))
                    sp.dma_start(dram_chunk(out, it, j), xs[:, j % RING]).then_inc(stored, 16)
                    sp.wait_ge(stored, count(it, stored, 16 * (j + 1)))
                if it.has(-1):
                    j = it.i + 1
                    sp.dma_start(xs[:, j % RING], dram_chunk(x, it, j)).then_inc(x_in[j % RING], 16)
                if it.has(1):
                    for group in (2, 3):
                        sp.wait_ge(dbx_ready, count(it, dbx_ready, N * (it.i - 1) + BG * (group - 1)))
                        load_b(it.i - 1, group)
                if it.has(0):
                    j = it.i
                    sp.wait_ge(*read_through(it, j, "P", 0))
                    sp.dma_start(scratch[j % 2, 0:N // 2], bc_t[0:N // 2, :]).then_inc(scratch_in, 16)
                    if (at := count(it, dbx_ready, N * j - BG)) is not None:
                        sp.wait_ge(dbx_ready, at)
                    sp.dma_start(scratch[j % 2, N // 2:N], bc_t[N // 2:N, :]).then_inc(scratch_in, 16)
                    sp.wait_ge(scratch_in, count(it, scratch_in, 32 * (j + 1)))
                    load_b(j, 0)
                    if (at := count(it, dbx_ready, N * j)) is not None:
                        sp.wait_ge(dbx_ready, at)
                    load_b(j, 1)

            program(sp, body)
            sp.wait_ge(stored, 16 * chunks)

        @block.gpsimd
        def _(pool):
            pool.memset(zero[:], 0.0)
            pool.memset(eps[:], EPS)
            pool.memset(minus_half[:], -0.5)
            pool.memset(minus_one[:], -1.0)
            pool.memset(ones[:], 1.0)
            pool.memset(mixed[:, :, :, :, T:T + 1], 0.0)
            pool.wait_ge(weights_in, WEIGHTS_LOADED)
            pool.tensor_scalar(one_mu[:], mu[:], -1.0, 1.0, ALU.mult, ALU.add)
            pool.tensor_scalar(w_v[:], w_v[:], 0.25, None, ALU.mult)
            pool.wait_ge(a_exp, 1)
            pool.tensor_scalar(neg_a[:], neg_a[:], -1.0, None, ALU.mult).then_inc(consts, 1)

            def scale_and_shift(it, j, kind):
                pool.wait_ge(stats_ready[kind], count(it, stats_ready[kind], TT * (j + 1)))
                if (at := count(it, normed[kind], TT * j)) is not None:
                    pool.wait_ge(normed[kind], at)
                pool.tensor_tensor(rstd[:, kind], mean_var[:, kind, :, 1], eps[:], ALU.add).then_inc(
                    small[kind], 1)
                pool.tensor_tensor(shift[:, kind], mean_var[:, kind, :, 0], minus_one[:], ALU.mult).then_inc(
                    small[kind], 1)
                pool.wait_ge(small[kind], count(it, small[kind], 4 * j + 2))
                pool.tensor_tensor(rstd[:, kind], rstd[:, kind], minus_half[:], ALU.pow).then_inc(small[kind], 1)
                pool.wait_ge(small[kind], count(it, small[kind], 4 * j + 3))
                pool.tensor_tensor(shift[:, kind], shift[:, kind], rstd[:, kind], ALU.mult).then_inc(
                    small[kind], 1)

            def add(it, j, which, t):
                pool.wait_ge(*read_through(it, j, "V" + which, t))
                pool.tensor_tensor(xs[:, j % RING, t], xs[:, j % RING, t], gated[:, t % 2], ALU.add).then_inc(
                    x_added, 1)

            def step_sizes(it, j):
                for g in range(DG):
                    pool.wait_ge(log_done, count(it, log_done, DG * j + g + 1))
                    pool.tensor_tensor(dt[:, j % 2, g], dt[:, j % 2, g], relu_z[:, g], ALU.add).then_inc(
                        dt_ready, 1)

            def driving_terms(it, j):
                if (at := count(it, dbx_ready, N * j)) is not None:
                    pool.wait_ge(dbx_ready, at)
                for g in range(DG):
                    pool.wait_ge(dt_ready, count(it, dt_ready, DG * j + g + 1))
                    pool.tensor_tensor(u[:, g], dt[:, j % 2, g], z_t[:, g], ALU.mult).then_inc(u_ready, 1)

            def save_state(j, n):
                pool.tensor_tensor(state[:, n, :], h[:, n % 2, :, T - 1], ones[:], ALU.mult).then_inc(saved, 1)

            def drive(it, j, n):
                if (at := count(it, scanned, DG * (N * j + n - 1))) is not None:
                    pool.wait_ge(scanned, at)
                if n >= 2:
                    save_state(j, n - 2)
                elif j > 0:
                    save_state(j - 1, n - 2 + N)
                if n == 0:
                    pool.wait_ge(u_ready, count(it, u_ready, DG * (j + 1)))
                if n % BG == 0:
                    group = n // BG
                    pool.wait_ge(b_in[group % 2], count(it, b_in[group % 2], 32 * j + 16 * (group // 2 + 1)))
                b_n = b_all[:, (n // BG) % 2, n % BG].unsqueeze(1).broadcast_to([P, DG, T])
                pool.tensor_tensor(dbx[:, n % 2], u[:], b_n, ALU.mult).then_inc(dbx_ready, 1)

            def body(it):
                for slot in range(N):
                    if it.has(1):
                        drive(it, it.i - 1, slot)
                    for what, k, _, j in it.due(pool_share[slot]):
                        if what[0] == "A":
                            add(it, j, what[1], k)
                        if what[0] == "N":
                            scale_and_shift(it, j, KIND[what[1]])
                        if what == "dt":
                            step_sizes(it, j)
                if it.has(0):
                    driving_terms(it, it.i)

            program(pool, body)

        @block.scalar
        def _(act):
            act.wait_ge(weights_in, WEIGHTS_LOADED)
            act.activation(neg_a[:], neg_a[:], ACT.Exp).then_inc(a_exp, 1)
            act.wait_ge(consts, 2)

            def decay(it, j, unit):
                n, g = unit // DG, unit % DG
                if n == 0:
                    act.wait_ge(dt_ready, count(it, dt_ready, DG * j + g + 1))
                if (at := count(it, scanned, N * DG * j + unit - 1)) is not None:
                    act.wait_ge(scanned, at)
                act.activation(dec[:, unit % 2], dt[:, j % 2, g], ACT.Exp,
                               scale=neg_a[:, g, n:n + 1]).then_inc(dec_ready, 1)

            def first_x_prev(it, j, kind):
                q = ffn_number(kind, j)
                if j > 0:
                    act.wait_ge(turned, count(it, turned, DG * (ffn_number(kind, j - 1) + 1)))
                for rk in range(2):
                    ins = act.copy(mixed[:, kind, rk, :, 0],
                                   zero[:] if j % PER_BATCH == 0 else mixed[:, kind, rk, :, T])
                ins.then_inc(carried, 1)
                act.wait_ge(carried, count(it, carried, q + 1))

            def read_bank(it, j, piece, k, step):
                b = bank(j, piece, k)
                src, free, what = ring[:, b], done[b], piece[0]
                if step == 0:
                    if what == "T" and k == 0:
                        first_x_prev(it, j, KIND[piece[1]])
                    if what == "Z" and k == 0:
                        if (at := count(it, u_ready, DG * j)) is not None:
                            act.wait_ge(u_ready, at)
                    if what == "P":
                        if (at := count(it, scratch_in, 32 * j)) is not None:
                            act.wait_ge(scratch_in, at)
                    if what == "C":
                        if (at := count(it, summed, N * TT * (j - 1))) is not None:
                            act.wait_ge(summed, at)
                    act.wait_ge(*bank_filled(it, j, piece, k))
                if what == "T":
                    ins = act.activation(mixed[:, KIND[piece[1]], step, k, 1:T + 1], src, ACT.Copy,
                                         scale=one_mu[:, step, k:k + 1])
                    if step == 1:
                        ins.then_inc(turned, 1)
                elif what == "K" and step == 0:
                    act.activation(key[:, k], src, ACT.Relu).then_inc(free, 1)
                elif what == "K":
                    act.wait_ge(*read_through(it, j, piece, k))
                    act.activation(key[:, k], key[:, k], ACT.Square).then_inc(squared, 1)
                elif what == "R":
                    act.activation(gate[:, k], src, ACT.Tanh, scale=0.5).then_inc(free, 1)
                elif what == "Z":
                    act.copy(z_t[:, k], src).then_inc(free, 1)
                elif what == "P" and step == 0:
                    act.activation(dt_r[0:RANK, :], src[0:RANK], ACT.Identity, bias=b_x[0:RANK])
                elif what == "P":
                    act.activation(bc_t[:], src[RANK:PROJ], ACT.Identity, bias=b_x[RANK:PROJ]).then_inc(free, 1)
                elif what == "C":
                    act.copy(bc_tok[:, j % 2], src[:, 0:TT * 2 * N].rearrange("p (t c) -> p t c", t=TT)).then_inc(
                        free, 1)
                elif what == "D" and step == 0:
                    act.activation(dt[:, j % 2, k], src, ACT.Abs)
                elif what == "D":
                    act.activation(relu_z[:, k], src, ACT.Relu).then_inc(free, 1)

            def normalize(it, j, kind, t, phase):
                if t == 0:
                    act.wait_ge(small[kind], count(it, small[kind], 4 * (j + 1)))
                    if (at := count(it, filled, transposed_before(it, phase))) is not None:
                        act.wait_ge(filled, at)
                act.activation(xn[:, t], xs[:, j % RING, t], ACT.Identity, scale=rstd[:, kind, t:t + 1],
                               bias=shift[:, kind, t:t + 1]).then_inc(normed[kind], 1)

            def exponential(it, j, g):
                act.wait_ge(*read_through(it, j, "D", g))
                act.activation(dt[:, j % 2, g], dt[:, j % 2, g], ACT.Exp, scale=-1.0).then_inc(exp_done, 1)

            def logarithms(it, j):
                for g in range(DG):
                    act.wait_ge(exp_done, count(it, exp_done, DG * j + g + 1))
                    act.activation(dt[:, j % 2, g], dt[:, j % 2, g], ACT.Ln, bias=1.0).then_inc(log_done, 1)

            def body(it):
                for phase in range(PHASES):
                    if phase + AHEAD < PHASES and it.has(1):
                        decay(it, it.i - 1, phase + AHEAD)
                    if phase + AHEAD >= PHASES and it.has(0):
                        decay(it, it.i, phase + AHEAD - PHASES)
                    for piece, k, step, j in it.due(act_share[phase]):
                        if piece == "E":
                            exponential(it, j, k)
                        elif piece == "L":
                            logarithms(it, j)
                        elif piece[0] == "N":
                            normalize(it, j, KIND[piece[1]], step, phase)
                        else:
                            read_bank(it, j, piece, k, step)

            program(act, body)

        @block.vector
        def _(dve):
            dve.memset(dt_r[RANK:RANK + 1, :], 1.0).then_inc(consts, 1)
            dve.wait_ge(consts, 2)

            def scan(it, j, n, g):
                unit = n * DG + g
                if g == 0:
                    dve.wait_ge(dbx_ready, count(it, dbx_ready, N * j + n + 1))
                    if (at := count(it, h_turned, TT * (N * j + n - 1))) is not None:
                        dve.wait_ge(h_turned, at)
                    if (at := count(it, saved, N * j + n - 1)) is not None:
                        dve.wait_ge(saved, at)
                dve.wait_ge(dec_ready, count(it, dec_ready, N * DG * j + unit + 1))
                dve.tensor_tensor_scan(h[:, n % 2, g], dec[:, unit % 2], dbx[:, n % 2, g],
                                       0.0 if j % PER_BATCH == 0 else state[:, n, g:g + 1],
                                       ALU.mult, ALU.add).then_inc(scanned, 1)

            def sum_column(it, j, unit):
                m, t = unit // TT, unit % TT
                if m == 0 and t == 0:
                    dve.wait_ge(*read_through(it, j, "C", 0))
                    dve.wait_ge(normed[2], count(it, normed[2], TT * (j + 1)))
                dve.wait_ge(h_turned, count(it, h_turned, N * TT * j + unit + 1))
                if (at := count(it, summed, N * TT * j + unit - TT + 1)) is not None:
                    dve.wait_ge(summed, at)
                dve.scalar_tensor_tensor(
                    out=xs[:, j % RING, t], in0=h_tok[:, unit % 2], scalar=bc_tok[:, j % 2, t, N + m:N + m + 1],
                    in1=xs[:, j % RING, t], op0=ALU.mult, op1=ALU.add).then_inc(summed, 1)

            def statistics(it, j, kind, step):
                if step == 0 and kind == 0:
                    dve.wait_ge(x_in[j % RING], count(it, x_in[j % RING], 16 * (j // RING + 1)))
                if step == 0 and kind == 1:
                    dve.wait_ge(summed, count(it, summed, N * TT * (j + 1)))
                if step < TT and kind == 2:
                    dve.wait_ge(x_added, count(it, x_added, TT * ffn_number(0, j) + step + 1))
                if step < TT:
                    if (at := count(it, stats_ready[kind], TT * j)) is not None:
                        dve.wait_ge(stats_ready[kind], at)
                    dve.bn_stats(stats[:, kind, step], xs[:, j % RING, step]).then_inc(bn_done[kind], 1)
                else:
                    if (at := count(it, small[kind], 4 * j)) is not None:
                        dve.wait_ge(small[kind], at)
                    dve.wait_ge(bn_done[kind], count(it, bn_done[kind], TT * (j + 1)))
                    dve.memset(spare[:], 0.0)
                    for t in range(TT):
                        dve.bn_aggr(mean_var[:, kind, t], stats[:, kind, t]).then_inc(stats_ready[kind], 1)

            def mix(it, j, piece, k, step):
                kind, b = KIND[piece[1]], bank(j, piece, k)
                dve.wait_ge(turned, count(it, turned, DG * ffn_number(kind, j) + k + 1))
                dst = mixed[:, kind, step, k, 0:T]
                ins = dve.scalar_tensor_tensor(out=dst, in0=ring[:, b], scalar=mu[:, step, k:k + 1], in1=dst,
                                               op0=ALU.mult, op1=ALU.add)
                if step == 1:
                    ins.then_inc(done[b], 1)

            def gate_value(it, j, which, k):
                b = bank(j, "V" + which, k)
                dve.wait_ge(*bank_filled(it, j, "V" + which, k))
                dve.wait_ge(*read_through(it, j, "R" + which, k))
                if (at := count(it, x_added, TT * ffn_number(KIND[which], j) + k - 1)) is not None:
                    dve.wait_ge(x_added, at)
                dve.scalar_tensor_tensor(out=gated[:, k % 2], in0=gate[:, k], scalar=1.0, in1=ring[:, b],
                                         op0=ALU.add, op1=ALU.mult).then_inc(done[b], 1)

            def body(it):
                for phase in range(PHASES):
                    n, unit = phase // 4, phase % 4
                    if it.has(1):
                        scan(it, it.i - 1, n, unit)
                    if phase >= SUM_LATER and it.has(1):
                        sum_column(it, it.i - 1, phase - SUM_LATER)
                    if phase < SUM_LATER and it.has(2):
                        sum_column(it, it.i - 2, phase - SUM_LATER + PHASES)
                    for piece, k, step, j in it.due(dve_share[phase]):
                        if piece[0] == "S":
                            statistics(it, j, KIND[piece[1]], step)
                        if piece[0] == "T":
                            mix(it, j, piece, k, step)
                        if piece[0] == "V":
                            gate_value(it, j, piece[1], k)

            program(dve, body)

        @block.tensor
        def _(pe):
            pe.wait_ge(weights_in, WEIGHTS_LOADED)
            pe.wait_ge(consts, 2)

            def turn_h(it, j, m, t):
                unit = m * TT + t
                if t == 0:
                    pe.wait_ge(scanned, count(it, scanned, DG * (N * j + m + 1)))
                if (at := count(it, summed, N * TT * j + unit - 1)) is not None:
                    pe.wait_ge(summed, at)
                for g in range(DG):
                    ins = pe.transpose(h_tok[:, unit % 2, g * P:(g + 1) * P],
                                       h[:, m % 2, g, t * P:(t + 1) * P], eye[:])
                ins.then_inc(h_turned, 1)

            def operands(piece, k, c):
                cols = slice(k * P, (k + 1) * P)
                kind = KIND.get(piece[-1])
                if piece[0] == "K":
                    return w_k[:, c, cols], mixed[:, kind, 1, c, 0:T]
                if piece[0] == "R":
                    return mixed[:, kind, 0, c, cols], w_r[:, c]
                if piece[0] == "V":
                    return key[:, c, cols], w_v[:, c]
                return w_x[:, c], z_t[:, c]

            def fill_bank(it, j, piece, k, step):
                f, b = fills[j, piece, k], bank(j, piece, k)
                what, dst = piece[0], ring[:, bank(j, piece, k)]
                cols = slice(k * P, (k + 1) * P)
                if step == 0:
                    if (at := count(it, done[b], f // RING)) is not None:
                        pe.wait_ge(done[b], at)
                    if what in "TZ":
                        pe.wait_ge(normed[KIND[piece[-1]]], count(it, normed[KIND[piece[-1]]], TT * (j + 1)))
                    if what == "K" and k == 0:
                        pe.wait_ge(*read_through(it, j, "T" + piece[1], DG - 1))
                    if what == "V" and k == 0:
                        pe.wait_ge(squared, count(it, squared, DG * (ffn_number(KIND[piece[1]], j) + 1)))
                    if what == "P":
                        pe.wait_ge(*read_through(it, j, "Z", DG - 1))
                    if what == "C":
                        pe.wait_ge(*read_through(it, j, "P", 0))
                if what in "TZ":
                    for t in range(TT):
                        ins = pe.transpose(dst[:, t * P:(t + 1) * P], xn[:, t, cols], eye[:])
                elif what == "C":
                    for t in range(TT):
                        ins = pe.matmul(dst[:, t * 2 * N:(t + 1) * 2 * N], bc_t[:, t * P:(t + 1) * P],
                                        eye[0:2 * N, 0:2 * N], start=True, stop=True)
                elif what == "D":
                    ins = pe.matmul(dst, w_dt[:, cols], dt_r[:], start=True, stop=True)
                else:
                    stationary, moving = operands(piece, k, step)
                    ins = pe.matmul(dst[0:PROJ] if what == "P" else dst, stationary, moving,
                                    start=(step == 0), stop=(step == DG - 1))
                if step == PE_STEPS[what] - 1:
                    ins.then_inc(filled, 1)

            def body(it):
                for phase in range(PHASES):
                    n, unit = phase // 4, phase % 4
                    if n and it.has(1):
                        turn_h(it, it.i - 1, n - 1, unit)
                    if n == 0 and it.has(2):
                        turn_h(it, it.i - 2, N - 1, unit)
                    for piece, k, step, j in it.due(pe_share[phase]):
                        fill_bank(it, j, piece, k, step)

            program(pe, body)


def kernel(L0_attn_x, L0_attn_x_proj_w, L0_attn_x_proj_b, L0_attn_dt_proj_w, L0_attn_dt_proj_b, L0_attn_A_log,
           L0_ffn_W_r, L0_ffn_W_k, L0_ffn_W_v, L0_ffn_mu_r, L0_ffn_mu_k):
    import concourse.bacc as bacc
    import numpy as np
    from concourse.bass_utils import run_bass_kernel_spmd

    def rows(w):
        w = np.asarray(w)
        return np.ascontiguousarray(w.reshape(-1, P, w.shape[1]).transpose(1, 0, 2))

    x = np.asarray(L0_attn_x)
    batch, length, _ = x.shape
    assert length == 4 * T
    arrays = {
        "x": np.ascontiguousarray(x.reshape(batch * length // T, T, D)),
        "ident": np.eye(P, dtype=np.float32),
        "wr_t": rows(np.asarray(L0_ffn_W_r).T),
        "wk_t": rows(np.asarray(L0_ffn_W_k).T),
        "wv_t": rows(np.asarray(L0_ffn_W_v).T),
        "mu_r": np.ascontiguousarray(np.asarray(L0_ffn_mu_r).reshape(DG, P).T),
        "mu_k": np.ascontiguousarray(np.asarray(L0_ffn_mu_k).reshape(DG, P).T),
        "xp_t": rows(np.asarray(L0_attn_x_proj_w).T),
        "xp_b": np.ascontiguousarray(np.asarray(L0_attn_x_proj_b).reshape(PROJ, 1)),
        "dt_t": np.ascontiguousarray(np.asarray(L0_attn_dt_proj_w).T),
        "dt_b": np.ascontiguousarray(np.asarray(L0_attn_dt_proj_b).reshape(1, D)),
        "a_log": rows(np.asarray(L0_attn_A_log)),
    }
    nc = bacc.Bacc("TRN2", target_bir_lowering=False, num_devices=1)
    args = {name: nc.dram_tensor(f"in_{name}", a.shape, mybir.dt.from_np(a.dtype), kind="ExternalInput").ap()
            for name, a in arrays.items()}
    scratch = nc.dram_tensor("scratch_b", (2, N, T), F32, kind="Internal").ap()
    out = nc.dram_tensor("out_y", arrays["x"].shape, F32, kind="ExternalOutput").ap()
    macaron_kernel(nc, **args, scratch=scratch, out=out)
    got = run_bass_kernel_spmd(nc, [{f"in_{name}": a for name, a in arrays.items()}], core_ids=[0])
    return got.results[0]["out_y"].reshape(batch, length, D)
```

```python
from contextlib import ExitStack

import concourse.bass as bass
from concourse import mybir

F32 = mybir.dt.float32
F32R = mybir.dt.float32r
ALU = mybir.AluOpType
ACT = mybir.ActivationFunctionType

P = 128
T = 512
TT = T // P
D = 512
DG = D // P
N = 16
RANK = 64
PROJ = RANK + 2 * N
EPS = 1e-5
RING = 4
BG = 2

PER_BATCH = 4
WEIGHTS_LOADED = 16 * 11
AHEAD = 1
SUM_LATER = 4
PHASES = 4 * N


def some(piece, lag, *ks):
    return [(piece, k, lag) for k in ks]


ORDER = (some("K1", 0, 3) + some("R1", 0, 0, 1, 2, 3)
         + some("T2", 2, 0) + some("V1", 0, 0) + some("T2", 2, 1) + some("V1", 0, 1) + some("T2", 2, 2)
         + some("V1", 0, 2) + some("T2", 2, 3) + some("V1", 0, 3)
         + some("K2", 2, 0, 1, 2, 3)
         + some("R2", 2, 0) + some("Z", 0, 0, 1, 2, 3) + some("R2", 2, 1) + some("P", 0, 0) + some("R2", 2, 2)
         + some("C", 0, 0) + some("D", 0, 0, 1, 2, 3) + some("R2", 2, 3)
         + some("T1", -1, 0) + some("V2", 2, 0) + some("T1", -1, 1) + some("V2", 2, 1)
         + some("T1", -1, 2) + some("V2", 2, 2) + some("T1", -1, 3) + some("V2", 2, 3)
         + some("K1", -1, 0, 1, 2))
PE_COST = {"T": 0.8, "Z": 0.5, "C": 0.3, "V": 0.25}
PE_STEPS = {"T": 1, "Z": 1, "K": DG, "R": DG, "V": 3 * DG, "P": DG, "C": 1, "D": 1}
ACT_STEPS = {"T": 2, "Z": 1, "K": 3, "R": 1, "V": 0, "P": 2, "C": 1, "D": 2}
LATER = dict(T=0, Z=1, K=1, R=1, V=0, P=1, C=0, D=0, mix=1)
LOGARITHMS = 4
STATS_SLOT = 9
KIND = {"1": 0, "2": 1, "Z": 2}


def timetable():
    pe, act, dve = ([[] for _ in range(PHASES)] for _ in range(3))
    pool = [[] for _ in range(N)]
    begun_at, filled_at, read_at, split_at, normed_at = {}, {}, {}, {}, {}
    steps = [(lag, p, k, s) for p, k, lag in ORDER for s in range(PE_STEPS[p[0]])]
    costs = [PE_COST.get(p[0], 1.0) for _, p, _, _ in steps]
    for r, (lag, p, k, s) in enumerate(steps):
        phase = int(PHASES * sum(costs[:r]) / sum(costs))
        pe[phase].append((lag, p, k, s))
        begun_at.setdefault((p, k), lag * PHASES + phase)
        filled_at[p, k] = lag * PHASES + phase
    in_turn = sorted(filled_at, key=lambda piece: filled_at[piece] % PHASES)

    def place(table, at, *what, most=2):
        while len(table[at % PHASES]) >= most:
            at += 1
        table[at % PHASES].append((at // PHASES,) + what)
        return at

    def give_pool(at, what, k):
        slot = at // 4 + 1
        pool[slot % N].append((slot // N, what, k, 0))
        return 4 * slot - 1

    for p, k in in_turn:
        at = filled_at[p, k] + LATER[p[0]]
        for s in range(ACT_STEPS[p[0]]):
            at = place(act, at + (p[0] == "K" and s >= 1), p, k, s)
        read_at[p, k] = at
        if p == "D":
            at = place(act, at + 1, "E", k, 0)
        if (p, k) == ("D", DG - 1):
            at += LOGARITHMS
            act[at % PHASES].insert(0, (at // PHASES, "L", 0, 0))
            give_pool(at, "dt", 0)
        if p[0] == "K":
            split_at[p, k] = give_pool(at, "K" + p[1], k)
    for p, k in in_turn:
        if p[0] == "T":
            for s in range(2):
                read_at[p, k] = place(dve, read_at[p, k] + LATER["mix"] * (s == 0), p, k, s)
        if p[0] == "V":
            at = place(dve, max(filled_at[p, k], read_at["R" + p[1], k]) + LATER["V"], p, k, 0)
            read_at[p, k] = give_pool(at, "A" + p[1], k)
    for kind, at in (("2", 2 * PHASES + SUM_LATER), ("Z", read_at["V1", TT - 1] + 1), ("1", -PHASES + 4 * STATS_SLOT)):
        for s in range(TT + 1):
            if kind == "Z" and s < TT:
                at = read_at["V1", s] + 1
            at = place(dve, at, "S" + kind, 0, s)
        at = give_pool(at, "N" + kind, 0) + 2
        for s in range(TT):
            at = place(act, at, "N" + kind, 0, s, most=3)
        normed_at[kind] = at
    check_order(begun_at, filled_at, read_at, split_at, normed_at)
    return pe, act, dve, pool


def check_order(begun_at, filled_at, read_at, split_at, normed_at):
    for piece in ("T1", "T2", "Z"):
        kind = piece[-1]
        assert begun_at[piece, 0] > normed_at[kind], (piece, begun_at[piece, 0], normed_at[kind])
    for before, after, wrap in (("T2", "Z", 2), ("Z", "1", 1), ("T1", "2", -2)):
        gap = normed_at[after] - TT - filled_at[before, DG - 1] + wrap * PHASES
        assert gap > 0, (before, after, gap)
    for which in "12":
        assert begun_at["K" + which, 0] > max(read_at["T" + which, g] for g in range(DG)), ("K", which)
        assert begun_at["V" + which, 0] > max(split_at["K" + which, g] for g in range(DG)), ("V", which)
    assert begun_at["P", 0] > max(read_at["Z", g] for g in range(DG))
    assert filled_at["C", 0] > read_at["P", 0]
    flat = [(p, k) for p, k, _ in ORDER]
    for new, old in zip(flat, flat[-RING:] + flat[:-RING]):
        begun = begun_at[new] % PHASES
        read = filled_at[old] % PHASES + read_at[old] - filled_at[old]
        assert begun + PHASES * (filled_at[old] % PHASES > begun) >= read - 1, (new, old)


class Step:

    def __init__(self, i, turn, chunks):
        self.i, self.turn, self.chunks = i, turn, chunks

    def has(self, lag):
        return 0 <= self.i - lag < self.chunks

    def due(self, entries):
        return [(p, k, s, self.i - lag) for lag, p, k, s in entries if self.has(lag)]


def bank_table(chunks):
    table = {}
    for i in range(-1, chunks + 3):
        for piece, k, lag in ORDER:
            if 0 <= i - lag < chunks:
                table[i - lag, piece, k] = len(table)
    return table


def macaron_kernel(nc, x, ident, wr_t, wk_t, wv_t, mu_r, mu_k, xp_t, xp_b, dt_t, dt_b, a_log, scratch, out):
    chunks = x.shape[0]
    fills = bank_table(chunks)
    pe_share, act_share, dve_share, pool_share = timetable()
    fills_per_chunk = len(ORDER)
    assert chunks % PER_BATCH == 0 and chunks >= 8 and (PER_BATCH * fills_per_chunk) % RING == 0

    with ExitStack() as ctx:
        def sb(name, shape):
            return ctx.enter_context(nc.sbuf_tensor(name, shape, F32))

        def ps(name, shape):
            return ctx.enter_context(nc.psum_tensor(name, shape, F32))

        rates = {}

        def sem(name, per_chunk=0):
            semaphore = ctx.enter_context(nc.semaphore(name))
            rates[semaphore.name] = per_chunk
            return semaphore

        eye = sb("eye", [P, P])
        w_r = sb("w_r", [P, DG, D])
        w_k = sb("w_k", [P, DG, D])
        w_v_high = sb("w_v_high", [P, DG, D])
        w_v_low = sb("w_v_low", [P, DG, D])
        w_x = sb("w_x", [P, DG, PROJ])
        w_dt = sb("w_dt", [RANK + 1, D])
        b_x = sb("b_x", [PROJ, 1])
        mu = sb("mu", [P, 2, DG])
        one_mu = sb("one_mu", [P, 2, DG])
        neg_a = sb("neg_a", [P, DG, N])
        zero = sb("zero", [P, 2, DG])
        eps = sb("eps", [P, TT])
        minus_half = sb("minus_half", [P, TT])
        minus_one = sb("minus_one", [P, TT])
        ones = sb("ones", [P, DG])

        xs = sb("xs", [P, RING, TT, D])
        xn = sb("xn", [P, TT, D])
        mixed = sb("mixed", [P, 2, DG, T + 1])
        carry = sb("carry", [P, 2, 2, DG])
        relu = sb("relu", [P, DG, T])
        key_high = sb("key_high", [P, DG, T])
        key_low = sb("key_low", [P, DG, T])
        gate = sb("gate", [P, TT, D])
        gated = sb("gated", [P, 2, D])
        z_t = sb("z_t", [P, DG, T])
        dt_r = sb("dt_r", [RANK + 1, T])
        bc_t = sb("bc_t", [2 * N, T])
        bc_tok = sb("bc_tok", [P, 2, TT, 2 * N])
        dt = sb("dt", [P, 2, DG, T])
        u = sb("u", [P, DG, T])
        b_all = sb("b_all", [P, 2, BG, T])
        dbx = sb("dbx", [P, 2, DG, T])
        h = sb("h", [P, 2, DG, T])
        w_v_raw = h[:, 0]
        state = sb("state", [P, N, DG])
        stats = sb("stats", [P, 3, TT, 6])
        mean_var = sb("mean_var", [P, 3, TT, 2])
        rstd = sb("rstd", [P, 3, TT])
        shift = sb("shift", [P, 3, TT])
        spare = sb("spare", [P, 1])

        ring = ps("ring", [P, RING, 512])
        dec = ps("dec", [P, 2, 512])
        h_tok = ps("h_tok", [P, 2, 512])

        weights_in = sem("weights_in")
        consts = sem("consts")
        v_scaled = sem("v_scaled")
        v_high = sem("v_high")
        a_exp = sem("a_exp")
        x_in = [sem(f"x_in{b}", 4) for b in range(RING)]
        stored = sem("stored", 16)
        scratch_in = sem("scratch_in", 32)
        b_in = [sem(f"b_in{b}", 16 * N // BG // 2) for b in range(2)]
        filled = sem("filled", fills_per_chunk)
        done = [sem(f"done{b}", fills_per_chunk / RING) for b in range(RING)]
        bn_done = [sem(f"bn_done{k}", TT) for k in range(3)]
        stats_ready = [sem(f"stats_ready{k}", TT) for k in range(3)]
        small = [sem(f"small{k}", 4) for k in range(3)]
        normed = [sem(f"normed{k}", TT) for k in range(3)]
        turned = sem("turned", 2 * DG)
        carried = sem("carried", 4)
        squared = sem("squared", 2 * DG)
        rounded = sem("rounded", 2 * DG)
        key_split = sem("key_split", 2 * DG)
        x_added = sem("x_added", 2 * TT)
        exp_done = sem("exp_done", DG)
        log_done = sem("log_done", DG)
        dt_ready = sem("dt_ready", DG)
        u_ready = sem("u_ready", DG)
        dbx_ready = sem("dbx_ready", N)
        saved = sem("saved", N)
        dec_ready = sem("dec_ready", N * DG)
        scanned = sem("scanned", N * DG)
        h_turned = sem("h_turned", N * TT)
        summed = sem("summed", N * TT)

        def count(it, semaphore, value):
            if it.turn is None:
                return value if value > 0 else None
            assert value > 0 and rates[semaphore.name] > 0
            return it.turn * int(PER_BATCH * rates[semaphore.name]) + value

        def ffn_number(kind, j):
            if kind == 0:
                return j if j <= 2 else 2 * j - 2
            return min(2 * j + 3, chunks + j)

        def bank(j, piece, k):
            return fills[j, piece, k] % RING

        def bank_filled(it, j, piece, k):
            return filled, count(it, filled, fills[j, piece, k] + 1)

        def read_through(it, j, piece, k):
            b = bank(j, piece, k)
            return done[b], count(it, done[b], fills[j, piece, k] // RING + 1)

        def transposed_before(it, phase):
            last = 0
            for i in (it.i - 1, it.i):
                for entries in pe_share[:phase if i == it.i else PHASES]:
                    for lag, piece, k, _ in entries:
                        if piece[0] in "TZ" and (i - lag, piece, k) in fills:
                            last = fills[i - lag, piece, k] + 1
            return last

        def program(eng, body):
            for i in range(-1, 3):
                body(Step(i, None, chunks))
            with eng.Fori(0, (chunks - PER_BATCH) // PER_BATCH) as turn:
                for i in range(3, 3 + PER_BATCH):
                    body(Step(i, turn, chunks))
            for i in range(chunks - 1, chunks + 3):
                body(Step(i, None, chunks))

        block = ctx.enter_context(nc.Block())

        @block.sync
        def _(sp):
            for dst, src in ((eye[:], ident), (mu[:, 0], mu_r), (mu[:, 1], mu_k), (b_x[:], xp_b),
                             (neg_a[:], a_log), (w_k[:], wk_t), (w_r[:], wr_t), (w_v_raw, wv_t), (w_x[:], xp_t),
                             (w_dt[0:RANK, :], dt_t), (w_dt[RANK:RANK + 1, :], dt_b)):
                sp.dma_start(dst, src).then_inc(weights_in, 16)

            def load_b(j, group):
                half = group % 2
                rows = scratch[j % 2, BG * group:BG * (group + 1), :].unsqueeze(0).broadcast_to([P, BG, T])
                sp.dma_start(b_all[:, half], rows).then_inc(b_in[half], 16)

            def dram_chunk(tensor, it, j):
                chunk = tensor[j] if it.turn is None else tensor[it.turn * PER_BATCH + j]
                return chunk.rearrange("(t p) d -> p t d", p=P)

            def body(it):
                if it.has(3):
                    j = it.i - 3
                    sp.wait_ge(x_added, count(it, x_added, TT * (ffn_number(1, j) + 1)))
                    sp.dma_start(dram_chunk(out, it, j), xs[:, j % RING]).then_inc(stored, 16)
                    sp.wait_ge(stored, count(it, stored, 16 * (j + 1)))
                if it.has(-1):
                    j = it.i + 1
                    sp.dma_start(xs[:, j % RING], dram_chunk(x, it, j)).then_inc(x_in[j % RING], 16)
                if it.has(1):
                    for group in range(2, N // BG):
                        sp.wait_ge(dbx_ready, count(it, dbx_ready, N * (it.i - 1) + BG * (group - 1)))
                        load_b(it.i - 1, group)
                if it.has(0):
                    j = it.i
                    sp.wait_ge(*read_through(it, j, "P", 0))
                    sp.dma_start(scratch[j % 2, 0:N // 2], bc_t[0:N // 2, :]).then_inc(scratch_in, 16)
                    if (at := count(it, dbx_ready, N * j - BG)) is not None:
                        sp.wait_ge(dbx_ready, at)
                    sp.dma_start(scratch[j % 2, N // 2:N], bc_t[N // 2:N, :]).then_inc(scratch_in, 16)
                    sp.wait_ge(scratch_in, count(it, scratch_in, 32 * (j + 1)))
                    load_b(j, 0)
                    if (at := count(it, dbx_ready, N * j)) is not None:
                        sp.wait_ge(dbx_ready, at)
                    load_b(j, 1)

            program(sp, body)
            sp.wait_ge(stored, 16 * chunks)

        @block.gpsimd
        def _(pool):
            pool.memset(zero[:], 0.0)
            pool.memset(eps[:], EPS)
            pool.memset(minus_half[:], -0.5)
            pool.memset(minus_one[:], -1.0)
            pool.memset(ones[:], 1.0)
            pool.memset(mixed[:, :, :, T:T + 1], 0.0)
            pool.wait_ge(weights_in, WEIGHTS_LOADED)
            pool.tensor_scalar(one_mu[:], mu[:], -1.0, 1.0, ALU.mult, ALU.add)
            pool.tensor_scalar(w_v_raw, w_v_raw, 0.25, None, ALU.mult).then_inc(v_scaled, 1)
            pool.wait_ge(v_high, 1)
            pool.tensor_tensor(w_v_low[:].bitcast(F32R), w_v_raw, w_v_high[:], ALU.subtract)
            pool.wait_ge(a_exp, 1)
            pool.tensor_scalar(neg_a[:], neg_a[:], -1.0, None, ALU.mult).then_inc(consts, 1)

            def scale_and_shift(it, j, kind):
                pool.wait_ge(stats_ready[kind], count(it, stats_ready[kind], TT * (j + 1)))
                if (at := count(it, normed[kind], TT * j)) is not None:
                    pool.wait_ge(normed[kind], at)
                pool.tensor_tensor(rstd[:, kind], mean_var[:, kind, :, 1], eps[:], ALU.add).then_inc(
                    small[kind], 1)
                pool.tensor_tensor(shift[:, kind], mean_var[:, kind, :, 0], minus_one[:], ALU.mult).then_inc(
                    small[kind], 1)
                pool.wait_ge(small[kind], count(it, small[kind], 4 * j + 2))
                pool.tensor_tensor(rstd[:, kind], rstd[:, kind], minus_half[:], ALU.pow).then_inc(small[kind], 1)
                pool.wait_ge(small[kind], count(it, small[kind], 4 * j + 3))
                pool.tensor_tensor(shift[:, kind], shift[:, kind], rstd[:, kind], ALU.mult).then_inc(
                    small[kind], 1)

            def add(it, j, which, t):
                pool.wait_ge(*read_through(it, j, "V" + which, t))
                pool.tensor_tensor(xs[:, j % RING, t], xs[:, j % RING, t], gated[:, t % 2], ALU.add).then_inc(
                    x_added, 1)

            def step_sizes(it, j):
                for g in range(DG):
                    pool.wait_ge(log_done, count(it, log_done, DG * j + g + 1))
                    pool.tensor_tensor(dt[:, j % 2, g], dt[:, j % 2, g], relu[:, g], ALU.add).then_inc(
                        dt_ready, 1)

            def split_key(it, j, which, k):
                pool.wait_ge(rounded, count(it, rounded, DG * ffn_number(KIND[which], j) + k + 1))
                pool.tensor_tensor(key_low[:, k].bitcast(F32R), relu[:, k], key_high[:, k], ALU.subtract).then_inc(
                    key_split, 1)

            def driving_terms(it, j):
                if (at := count(it, dbx_ready, N * j)) is not None:
                    pool.wait_ge(dbx_ready, at)
                for g in range(DG):
                    pool.wait_ge(dt_ready, count(it, dt_ready, DG * j + g + 1))
                    pool.tensor_tensor(u[:, g], dt[:, j % 2, g], z_t[:, g], ALU.mult).then_inc(u_ready, 1)

            def save_state(j, n):
                pool.tensor_tensor(state[:, n, :], h[:, n % 2, :, T - 1], ones[:], ALU.mult).then_inc(saved, 1)

            def drive(it, j, n):
                if (at := count(it, scanned, DG * (N * j + n - 1))) is not None:
                    pool.wait_ge(scanned, at)
                if n >= 2:
                    save_state(j, n - 2)
                elif j > 0:
                    save_state(j - 1, n - 2 + N)
                if n == 0:
                    pool.wait_ge(u_ready, count(it, u_ready, DG * (j + 1)))
                if n % BG == 0:
                    group = n // BG
                    pool.wait_ge(b_in[group % 2], count(it, b_in[group % 2], 16 * (N // BG // 2 * j + group // 2 + 1)))
                b_n = b_all[:, (n // BG) % 2, n % BG].unsqueeze(1).broadcast_to([P, DG, T])
                pool.tensor_tensor(dbx[:, n % 2], u[:], b_n, ALU.mult).then_inc(dbx_ready, 1)

            def body(it):
                for slot in range(N):
                    if it.has(1):
                        drive(it, it.i - 1, slot)
                    for what, k, _, j in it.due(pool_share[slot]):
                        if what[0] == "A":
                            add(it, j, what[1], k)
                        if what[0] == "K":
                            split_key(it, j, what[1], k)
                        if what[0] == "N":
                            scale_and_shift(it, j, KIND[what[1]])
                        if what == "dt":
                            step_sizes(it, j)
                if it.has(0):
                    driving_terms(it, it.i)

            program(pool, body)

        @block.scalar
        def _(act):
            act.wait_ge(weights_in, WEIGHTS_LOADED)
            act.activation(neg_a[:], neg_a[:], ACT.Exp).then_inc(a_exp, 1)
            act.wait_ge(v_scaled, 1)
            act.copy(w_v_high[:].bitcast(F32R), w_v_raw).then_inc(v_high, 1)
            act.wait_ge(consts, 2)

            def decay(it, j, unit):
                n, g = unit // DG, unit % DG
                if n == 0:
                    act.wait_ge(dt_ready, count(it, dt_ready, DG * j + g + 1))
                if (at := count(it, scanned, N * DG * j + unit - 1)) is not None:
                    act.wait_ge(scanned, at)
                act.activation(dec[:, unit % 2], dt[:, j % 2, g], ACT.Exp,
                               scale=neg_a[:, g, n:n + 1]).then_inc(dec_ready, 1)

            def first_x_prev(it, j, kind):
                q = ffn_number(kind, j)
                if kind == 0:
                    before = 1 if j > 2 else 0
                else:
                    before = 0 if j + 2 < chunks else 1
                if (at := count(it, turned, DG * q)) is not None:
                    act.wait_ge(turned, at)
                act.copy(carry[:, before], mixed[:, :, :, T]).then_inc(carried, 1)
                act.wait_ge(carried, count(it, carried, 2 * q + 1))
                act.copy(mixed[:, :, :, 0], zero[:] if j % PER_BATCH == 0 else carry[:, kind]).then_inc(carried, 1)
                act.wait_ge(carried, count(it, carried, 2 * q + 2))

            def read_bank(it, j, piece, k, step):
                b = bank(j, piece, k)
                src, free, what = ring[:, b], done[b], piece[0]
                if step == 0:
                    if what == "Z" and k == 0:
                        if (at := count(it, u_ready, DG * j)) is not None:
                            act.wait_ge(u_ready, at)
                    if what == "P":
                        if (at := count(it, scratch_in, 32 * j)) is not None:
                            act.wait_ge(scratch_in, at)
                    if what == "K" and k == 0 and KIND[piece[1]] == 0:
                        if (at := count(it, dt_ready, DG * j)) is not None:
                            act.wait_ge(dt_ready, at)
                    if what == "D" and k == 0:
                        last = ffn_number(1, j - 2) if j >= 2 else ffn_number(0, j)
                        act.wait_ge(key_split, count(it, key_split, DG * (last + 1)))
                    if what == "C":
                        if (at := count(it, summed, N * TT * (j - 1))) is not None:
                            act.wait_ge(summed, at)
                    act.wait_ge(*bank_filled(it, j, piece, k))
                    if what == "T" and k == 0:
                        first_x_prev(it, j, KIND[piece[1]])
                if what == "T":
                    ins = act.activation(mixed[:, step, k, 1:T + 1], src, ACT.Copy,
                                         scale=one_mu[:, step, k:k + 1])
                    if step == 1:
                        ins.then_inc(turned, 1)
                elif what == "K" and step == 0:
                    act.activation(relu[:, k], src, ACT.Relu).then_inc(free, 1)
                elif what == "K" and step == 2:
                    act.wait_ge(squared, count(it, squared, DG * ffn_number(KIND[piece[1]], j) + k + 1))
                    act.copy(key_high[:, k].bitcast(F32R), relu[:, k]).then_inc(rounded, 1)
                elif what == "K":
                    act.wait_ge(*read_through(it, j, piece, k))
                    act.activation(relu[:, k], relu[:, k], ACT.Square).then_inc(squared, 1)
                elif what == "R":
                    act.activation(gate[:, k], src, ACT.Tanh, scale=0.5).then_inc(free, 1)
                elif what == "Z":
                    act.copy(z_t[:, k], src).then_inc(free, 1)
                elif what == "P" and step == 0:
                    act.activation(dt_r[0:RANK, :], src[0:RANK], ACT.Identity, bias=b_x[0:RANK])
                elif what == "P":
                    act.activation(bc_t[:], src[RANK:PROJ], ACT.Identity, bias=b_x[RANK:PROJ]).then_inc(free, 1)
                elif what == "C":
                    act.copy(bc_tok[:, j % 2], src[:, 0:TT * 2 * N].rearrange("p (t c) -> p t c", t=TT)).then_inc(
                        free, 1)
                elif what == "D" and step == 0:
                    act.activation(dt[:, j % 2, k], src, ACT.Abs)
                elif what == "D":
                    act.activation(relu[:, k], src, ACT.Relu).then_inc(free, 1)

            def normalize(it, j, kind, t, phase):
                if t == 0:
                    act.wait_ge(small[kind], count(it, small[kind], 4 * (j + 1)))
                    if (at := count(it, filled, transposed_before(it, phase))) is not None:
                        act.wait_ge(filled, at)
                act.activation(xn[:, t], xs[:, j % RING, t], ACT.Identity, scale=rstd[:, kind, t:t + 1],
                               bias=shift[:, kind, t:t + 1]).then_inc(normed[kind], 1)

            def exponential(it, j, g):
                act.wait_ge(*read_through(it, j, "D", g))
                act.activation(dt[:, j % 2, g], dt[:, j % 2, g], ACT.Exp, scale=-1.0).then_inc(exp_done, 1)

            def logarithms(it, j):
                for g in range(DG):
                    act.wait_ge(exp_done, count(it, exp_done, DG * j + g + 1))
                    act.activation(dt[:, j % 2, g], dt[:, j % 2, g], ACT.Ln, bias=1.0).then_inc(log_done, 1)

            def body(it):
                for phase in range(PHASES):
                    if phase + AHEAD < PHASES and it.has(1):
                        decay(it, it.i - 1, phase + AHEAD)
                    if phase + AHEAD >= PHASES and it.has(0):
                        decay(it, it.i, phase + AHEAD - PHASES)
                    for piece, k, step, j in it.due(act_share[phase]):
                        if piece == "E":
                            exponential(it, j, k)
                        elif piece == "L":
                            logarithms(it, j)
                        elif piece[0] == "N":
                            normalize(it, j, KIND[piece[1]], step, phase)
                        else:
                            read_bank(it, j, piece, k, step)

            program(act, body)

        @block.vector
        def _(dve):
            dve.memset(dt_r[RANK:RANK + 1, :], 1.0).then_inc(consts, 1)
            dve.wait_ge(consts, 2)

            def scan(it, j, n, g):
                unit = n * DG + g
                if g == 0:
                    dve.wait_ge(dbx_ready, count(it, dbx_ready, N * j + n + 1))
                    if (at := count(it, h_turned, TT * (N * j + n - 1))) is not None:
                        dve.wait_ge(h_turned, at)
                    if (at := count(it, saved, N * j + n - 1)) is not None:
                        dve.wait_ge(saved, at)
                dve.wait_ge(dec_ready, count(it, dec_ready, N * DG * j + unit + 1))
                dve.tensor_tensor_scan(h[:, n % 2, g], dec[:, unit % 2], dbx[:, n % 2, g],
                                       0.0 if j % PER_BATCH == 0 else state[:, n, g:g + 1],
                                       ALU.mult, ALU.add).then_inc(scanned, 1)

            def sum_column(it, j, unit):
                m, t = unit // TT, unit % TT
                if m == 0 and t == 0:
                    dve.wait_ge(*read_through(it, j, "C", 0))
                    dve.wait_ge(normed[2], count(it, normed[2], TT * (j + 1)))
                dve.wait_ge(h_turned, count(it, h_turned, N * TT * j + unit + 1))
                if (at := count(it, summed, N * TT * j + unit - TT + 1)) is not None:
                    dve.wait_ge(summed, at)
                dve.scalar_tensor_tensor(
                    out=xs[:, j % RING, t], in0=h_tok[:, unit % 2], scalar=bc_tok[:, j % 2, t, N + m:N + m + 1],
                    in1=xs[:, j % RING, t], op0=ALU.mult, op1=ALU.add).then_inc(summed, 1)

            def statistics(it, j, kind, step):
                if step == 0 and kind == 0:
                    dve.wait_ge(x_in[j % RING], count(it, x_in[j % RING], 16 * (j // RING + 1)))
                if step == 0 and kind == 1:
                    dve.wait_ge(summed, count(it, summed, N * TT * (j + 1)))
                if step < TT and kind == 2:
                    dve.wait_ge(x_added, count(it, x_added, TT * ffn_number(0, j) + step + 1))
                if step < TT:
                    if (at := count(it, stats_ready[kind], TT * j)) is not None:
                        dve.wait_ge(stats_ready[kind], at)
                    dve.bn_stats(stats[:, kind, step], xs[:, j % RING, step]).then_inc(bn_done[kind], 1)
                else:
                    if (at := count(it, small[kind], 4 * j)) is not None:
                        dve.wait_ge(small[kind], at)
                    dve.wait_ge(bn_done[kind], count(it, bn_done[kind], TT * (j + 1)))
                    dve.memset(spare[:], 0.0)
                    for t in range(TT):
                        dve.bn_aggr(mean_var[:, kind, t], stats[:, kind, t]).then_inc(stats_ready[kind], 1)

            def mix(it, j, piece, k, step):
                kind, b = KIND[piece[1]], bank(j, piece, k)
                dve.wait_ge(turned, count(it, turned, DG * ffn_number(kind, j) + k + 1))
                dst = mixed[:, step, k, 0:T]
                ins = dve.scalar_tensor_tensor(out=dst, in0=ring[:, b], scalar=mu[:, step, k:k + 1], in1=dst,
                                               op0=ALU.mult, op1=ALU.add)
                if step == 1:
                    ins.then_inc(done[b], 1)

            def gate_value(it, j, which, k):
                b = bank(j, "V" + which, k)
                dve.wait_ge(*bank_filled(it, j, "V" + which, k))
                dve.wait_ge(*read_through(it, j, "R" + which, k))
                if (at := count(it, x_added, TT * ffn_number(KIND[which], j) + k - 1)) is not None:
                    dve.wait_ge(x_added, at)
                dve.scalar_tensor_tensor(out=gated[:, k % 2], in0=gate[:, k], scalar=1.0, in1=ring[:, b],
                                         op0=ALU.add, op1=ALU.mult).then_inc(done[b], 1)

            def body(it):
                for phase in range(PHASES):
                    n, unit = phase // 4, phase % 4
                    if it.has(1):
                        scan(it, it.i - 1, n, unit)
                    if phase >= SUM_LATER and it.has(1):
                        sum_column(it, it.i - 1, phase - SUM_LATER)
                    if phase < SUM_LATER and it.has(2):
                        sum_column(it, it.i - 2, phase - SUM_LATER + PHASES)
                    for piece, k, step, j in it.due(dve_share[phase]):
                        if piece[0] == "S":
                            statistics(it, j, KIND[piece[1]], step)
                        if piece[0] == "T":
                            mix(it, j, piece, k, step)
                        if piece[0] == "V":
                            gate_value(it, j, piece[1], k)

            program(dve, body)

        @block.tensor
        def _(pe):
            pe.wait_ge(weights_in, WEIGHTS_LOADED)
            pe.wait_ge(consts, 2)

            def turn_h(it, j, m, t):
                unit = m * TT + t
                if t == 0:
                    pe.wait_ge(scanned, count(it, scanned, DG * (N * j + m + 1)))
                if (at := count(it, summed, N * TT * j + unit - 1)) is not None:
                    pe.wait_ge(summed, at)
                for g in range(DG):
                    ins = pe.transpose(h_tok[:, unit % 2, g * P:(g + 1) * P],
                                       h[:, m % 2, g, t * P:(t + 1) * P], eye[:])
                ins.then_inc(h_turned, 1)

            def operands(piece, k, step):
                c, part = step % DG, step // DG
                cols = slice(k * P, (k + 1) * P)
                if piece[0] == "K":
                    return w_k[:, c, cols], mixed[:, 1, c, 0:T]
                if piece[0] == "R":
                    return mixed[:, 0, c, cols], w_r[:, c]
                if piece[0] == "V":
                    return ((key_low if part == 1 else key_high)[:, c, cols].bitcast(F32R),
                            (w_v_low if part == 2 else w_v_high)[:, c].bitcast(F32R))
                return w_x[:, c], z_t[:, c]

            def fill_bank(it, j, piece, k, step):
                f, b = fills[j, piece, k], bank(j, piece, k)
                what, dst = piece[0], ring[:, bank(j, piece, k)]
                cols = slice(k * P, (k + 1) * P)
                if step == 0:
                    if (at := count(it, done[b], f // RING)) is not None:
                        pe.wait_ge(done[b], at)
                    if what in "TZ":
                        pe.wait_ge(normed[KIND[piece[-1]]], count(it, normed[KIND[piece[-1]]], TT * (j + 1)))
                    if what == "K" and k == 0:
                        pe.wait_ge(*read_through(it, j, "T" + piece[1], DG - 1))
                    if what == "V" and k == 0:
                        pe.wait_ge(key_split, count(it, key_split, DG * (ffn_number(KIND[piece[1]], j) + 1)))
                    if what == "P":
                        pe.wait_ge(*read_through(it, j, "Z", DG - 1))
                    if what == "C":
                        pe.wait_ge(*read_through(it, j, "P", 0))
                if what in "TZ":
                    for t in range(TT):
                        ins = pe.transpose(dst[:, t * P:(t + 1) * P], xn[:, t, cols], eye[:])
                elif what == "C":
                    for t in range(TT):
                        ins = pe.matmul(dst[:, t * 2 * N:(t + 1) * 2 * N], bc_t[:, t * P:(t + 1) * P],
                                        eye[0:2 * N, 0:2 * N], start=True, stop=True)
                elif what == "D":
                    ins = pe.matmul(dst, w_dt[:, cols], dt_r[:], start=True, stop=True)
                else:
                    stationary, moving = operands(piece, k, step)
                    ins = pe.matmul(dst[0:PROJ] if what == "P" else dst, stationary, moving,
                                    start=(step == 0), stop=(step == PE_STEPS[what] - 1))
                if step == PE_STEPS[what] - 1:
                    ins.then_inc(filled, 1)

            def body(it):
                for phase in range(PHASES):
                    n, unit = phase // 4, phase % 4
                    if n and it.has(1):
                        turn_h(it, it.i - 1, n - 1, unit)
                    if n == 0 and it.has(2):
                        turn_h(it, it.i - 2, N - 1, unit)
                    for piece, k, step, j in it.due(pe_share[phase]):
                        fill_bank(it, j, piece, k, step)

            program(pe, body)


def kernel(L0_attn_x, L0_attn_x_proj_w, L0_attn_x_proj_b, L0_attn_dt_proj_w, L0_attn_dt_proj_b, L0_attn_A_log,
           L0_ffn_W_r, L0_ffn_W_k, L0_ffn_W_v, L0_ffn_mu_r, L0_ffn_mu_k):
    import concourse.bacc as bacc
    import numpy as np
    from concourse.bass_utils import run_bass_kernel_spmd

    def rows(w):
        w = np.asarray(w)
        return np.ascontiguousarray(w.reshape(-1, P, w.shape[1]).transpose(1, 0, 2))

    x = np.asarray(L0_attn_x)
    batch, length, _ = x.shape
    assert length == 4 * T
    arrays = {
        "x": np.ascontiguousarray(x.reshape(batch * length // T, T, D)),
        "ident": np.eye(P, dtype=np.float32),
        "wr_t": rows(np.asarray(L0_ffn_W_r).T),
        "wk_t": rows(np.asarray(L0_ffn_W_k).T),
        "wv_t": rows(np.asarray(L0_ffn_W_v).T),
        "mu_r": np.ascontiguousarray(np.asarray(L0_ffn_mu_r).reshape(DG, P).T),
        "mu_k": np.ascontiguousarray(np.asarray(L0_ffn_mu_k).reshape(DG, P).T),
        "xp_t": rows(np.asarray(L0_attn_x_proj_w).T),
        "xp_b": np.ascontiguousarray(np.asarray(L0_attn_x_proj_b).reshape(PROJ, 1)),
        "dt_t": np.ascontiguousarray(np.asarray(L0_attn_dt_proj_w).T),
        "dt_b": np.ascontiguousarray(np.asarray(L0_attn_dt_proj_b).reshape(1, D)),
        "a_log": rows(np.asarray(L0_attn_A_log)),
    }
    nc = bacc.Bacc("TRN2", target_bir_lowering=False, num_devices=1)
    args = {name: nc.dram_tensor(f"in_{name}", a.shape, mybir.dt.from_np(a.dtype), kind="ExternalInput").ap()
            for name, a in arrays.items()}
    scratch = nc.dram_tensor("scratch_b", (2, N, T), F32, kind="Internal").ap()
    out = nc.dram_tensor("out_y", arrays["x"].shape, F32, kind="ExternalOutput").ap()
    macaron_kernel(nc, **args, scratch=scratch, out=out)
    got = run_bass_kernel_spmd(nc, [{f"in_{name}": a for name, a in arrays.items()}], core_ids=[0])
    return got.results[0]["out_y"].reshape(batch, length, D)
```
